# Optimizing a Trainium2 kernel written in Bass

```python
import numpy as np
import jax
import jax.numpy as jnp

def _softmax(x, axis=-1):
    return jax.nn.softmax(x, axis=axis)

def _gelu(x):
    return jax.nn.gelu(x, approximate=True)

def _silu(x):
    return jax.nn.silu(x)

def _sigmoid(x):
    return jax.nn.sigmoid(x)

def _layernorm(x, axis=-1, eps=1e-05):
    m = jnp.mean(x, axis=axis, keepdims=True)
    v = jnp.var(x, axis=axis, keepdims=True)
    return (x - m) / jnp.sqrt(v + eps)

def _scatter_add(tgt, idx, src, axis=0):
    return tgt.at[idx].add(src)

def _segment_sum(src, seg, n):
    return jax.ops.segment_sum(src, seg, n)
kernel_name = 'mk_adj_resnorm_d1_adj_r2_e441b4'

def setup_inputs(seed: int=0):
    np.random.seed(seed)
    _w = jnp.asarray

    def _rec_inputs():
        import jax
        import jax.numpy as jnp
        _gk = jax.random.key(seed)
        x = 7.22e-05 + 1 * jax.random.normal(jax.random.fold_in(_gk, 1), (8, 1024, 256), jnp.float32)
        _a = jax.random.bernoulli(jax.random.fold_in(_gk, 2), 0.0078125, (1024, 1024))
        _a = jnp.logical_or(_a, jnp.swapaxes(_a, -1, -2))
        _a = jnp.logical_or(_a, jnp.eye(1024, dtype=bool))
        _af = _a.astype(jnp.float32)
        adj = _af
        return (x, adj)
    x, adj = _rec_inputs()

    def _L0_gnn_setup():
        import jax, jax.numpy as jnp
        import numpy as np
        B, N, D = (8, 1024, 256)
        key = jax.random.key(seed)
        k1, k2, k3, k4, k5 = jax.random.split(key, 5)
        neuron_states = jax.random.normal(k1, (B, N, D), dtype=jnp.float32)
        adjacency = jax.random.randint(k2, (N, N), 0, 2).astype(jnp.float32)
        scale = 1.0 / np.sqrt(D)
        Wq = jax.random.normal(k3, (D, D), dtype=jnp.float32) * scale
        Wk = jax.random.normal(k4, (D, D), dtype=jnp.float32) * scale
        Wv = jax.random.normal(k5, (D, D), dtype=jnp.float32) * scale
        return {'neuron_states': neuron_states, 'adjacency': adjacency, 'Wq': Wq, 'Wk': Wk, 'Wv': Wv}
    _L0_gnn_all = _L0_gnn_setup()
    _L0_gnn_in = {k: v for k, v in _L0_gnn_all.items() if k in ('Wq', 'Wk', 'Wv')}
    del _L0_gnn_all
    return {'x': x, 'adj': adj, 'L0_gnn_Wq': _L0_gnn_in['Wq'], 'L0_gnn_Wk': _L0_gnn_in['Wk'], 'L0_gnn_Wv': _L0_gnn_in['Wv']}

def reference(x, adj, L0_gnn_Wq, L0_gnn_Wk, L0_gnn_Wv):
    import jax
    import jax.numpy as jnp

    def _L0_gnn_ref(neuron_states, adjacency, Wq, Wk, Wv):
        import jax, jax.numpy as jnp
        import numpy as np
        B, N, D = (8, 1024, 256)
        q = jnp.einsum('bnd,ed->bne', neuron_states, Wq)
        k = jnp.einsum('bnd,ed->bne', neuron_states, Wk)
        v = jnp.einsum('bnd,ed->bne', neuron_states, Wv)
        rel = jnp.einsum('bnd,bmd->bnm', q, k)
        rel = adjacency.T[None, :, :] * rel
        rel = rel / jnp.linalg.norm(rel, axis=2, keepdims=True)
        return jnp.einsum('bnm,bmd->bnd', rel, v)
    x = _layernorm(x + _L0_gnn_ref(x, adj, L0_gnn_Wq, L0_gnn_Wk, L0_gnn_Wv), axis=-1)
    return x

_drawn_inputs = setup_inputs


def setup_inputs(seed=0):
    import zlib

    import numpy as np

    out = dict(_drawn_inputs(seed))
    spreads = {}
    factors = {}
    for name, (base, spread) in spreads.items():
        noise = np.random.default_rng([zlib.crc32(name.encode()), seed]).standard_normal(out[name].shape)
        drawn = base * np.exp(spread * noise) if base else spread * noise
        out[name] = jnp.asarray(drawn.astype(out[name].dtype))
    for name, factor in factors.items():
        out[name] = (out[name] * factor).astype(out[name].dtype)
    return out
```

```python
import numpy as np
import concourse.bass as bass
from concourse import mybir
from contextlib import ExitStack

F32 = mybir.dt.float32
F32R = mybir.dt.float32r
ALU = mybir.AluOpType
ACT = mybir.ActivationFunctionType

B, N, D = 8, 1024, 256
P = 128
KT = D // P
MT = N // P
HALF = N // 2
NT = HALF // P
UNITS = 2 * B
RING = 4
PH = 4
UT = PH + MT
ADDS = MT - 1
EPS = 1e-5
PEEL = 2
BODY = 4
TRIPS = (UNITS - PEEL - 2) // BODY
assert PEEL + BODY * TRIPS == UNITS - 2 and UT % RING == 0


def run_units(eng, unit):
    for u in range(PEEL):
        unit(u, u)
    with eng.Fori(0, TRIPS) as i:
        for s in range(BODY):
            unit(i * BODY + (PEEL + s), (PEEL + s) % BODY)
    for u in range(UNITS - 2, UNITS):
        unit(u, u % BODY)


def build(nc, x, xT, adj, wq, wk, wvT, out):
    ctx = ExitStack()
    with ctx:
        def sb(name, shape, dt=F32):
            return ctx.enter_context(nc.sbuf_tensor(name, shape, dt))

        def bank(name):
            return ctx.enter_context(nc.psum_tensor(name, [P, 512], F32))

        def sem(name):
            return ctx.enter_context(nc.semaphore(name))

        adj_sb = sb("adj_sb", [P, MT, N])
        xt_raw = sb("xt_raw", [P, KT, N])
        xt_hi = [sb(f"xt_hi{i}", [P, KT, N], F32R) for i in range(2)]
        xt_lo = [sb(f"xt_lo{i}", [P, KT, N], F32R) for i in range(2)]
        y_hi = sb("y_hi", [P, KT, N], F32R)
        y_lo = sb("y_lo", [P, KT, N], F32R)
        v_hl = sb("v_hl", [P, MT, 2, D], F32R)
        rel_hi = [sb(f"rel_hi{h}", [P, MT, HALF], F32R) for h in range(2)]
        rel_lo = [sb(f"rel_lo{h}", [P, MT, HALF], F32R) for h in range(2)]
        sq = [sb(f"sq{i}", [P, HALF]) for i in range(2)]
        sqsum = [sb(f"sqsum{h}", [P, HALF]) for h in range(2)]
        xo = [sb(f"xo{h}", [P, NT, D]) for h in range(2)]
        wq_sb = sb("wq_sb", [P, KT, D])
        wk_sb = sb("wk_sb", [P, KT, D])
        wv_raw = sb("wv_raw", [P, KT, D])
        wv_hl = sb("wv_hl", [P, KT, 2, D], F32R)
        g_hi = sb("g_hi", [P, KT, D], F32R)
        g_lo = sb("g_lo", [P, KT, D], F32R)
        ones = sb("ones", [P, 1])
        minus_half = sb("minus_half", [P, NT])
        normsq = [sb(f"normsq{h}", [P, NT]) for h in range(2)]
        rnorm = [sb(f"rnorm{h}", [P, NT]) for h in range(2)]
        stats = [sb(f"stats{i}", [P, 6]) for i in range(2)]
        meanvar = sb("meanvar", [P, NT, 2])
        var_eps = sb("var_eps", [P, NT])
        rstd = [sb(f"rstd{h}", [P, NT]) for h in range(2)]
        shift = [sb(f"shift{h}", [P, NT]) for h in range(2)]

        ring = [bank(f"ring{i}") for i in range(RING)]
        pv = [bank(f"pv{i}") for i in range(2)]
        norm_ps = bank("norm_ps")
        g_ps = bank("g_ps")

        wqk_in = sem("wqk_in")
        wv_in = sem("wv_in")
        adj_in = [sem(f"adj_in{m}") for m in range(MT)]
        xt_in = sem("xt_in")
        x_in = [sem(f"x_in{h}") for h in range(2)]
        stored = [sem(f"stored{h}") for h in range(2)]
        g_done = sem("g_done")
        g_hi_done = sem("g_hi_done")
        g_lo_done = sem("g_lo_done")
        wv_hi_done = sem("wv_hi_done")
        wv_lo_done = sem("wv_lo_done")
        ones_done = sem("ones_done")
        xt_hi_done = sem("xt_hi_done")
        xt0_lo_done = sem("xt0_lo_done")
        xt_lo_done = sem("xt_lo_done")
        tile_full = sem("tile_full")
        masked = sem("masked")
        hi_done = sem("hi_done")
        lo_done = sem("lo_done")
        squared = sem("squared")
        added = sem("added")
        norm_full = sem("norm_full")
        normsq_done = sem("normsq_done")
        rnorm_done = sem("rnorm_done")
        pv_full = sem("pv_full")
        x_added = sem("x_added")
        pv_free = sem("pv_free")
        stats_done = sem("stats_done")
        aggr_done = sem("aggr_done")
        var_done = sem("var_done")
        rstd_done = sem("rstd_done")
        shift_done = sem("shift_done")
        normalised = sem("normalised")

        def batch_rows(t, u, k):
            return t[bass.ds(u * HALF, HALF), :].rearrange("(t p) d -> p t d", p=P)

        x_rows = x.rearrange("b n d -> (b n) d")
        out_rows = out.rearrange("b n d -> (b n) d")
        xT_rows = xT.rearrange("b d n -> (b d) n")

        def half_of(t, h):
            return slice(h * HALF, (h + 1) * HALF)

        def piece(t, i):
            return t[:, i % KT, (i // KT) * HALF:(i // KT + 1) * HALF]

        block = ctx.enter_context(nc.Block())

        @block.sync
        def _(sp):
            def load_xt(b):
                sp.dma_start(xt_raw[:, :, :],
                             xT_rows[bass.ds(b * D, D), :].rearrange("(k p) n -> p k n", p=P)).then_inc(xt_in, 16)

            def load_x(u, k):
                sp.dma_start(xo[k % 2][:, :, :], batch_rows(x_rows, u, k)).then_inc(x_in[k % 2], 16)

            def store(u, k):
                sp.dma_start(batch_rows(out_rows, u, k), xo[k % 2][:, :, :]).then_inc(stored[k % 2], 16)

            sp.dma_start(wq_sb[:, :, :], wq.rearrange("(k p) d -> p k d", p=P)).then_inc(wqk_in, 16)
            sp.dma_start(wk_sb[:, :, :], wk.rearrange("(k p) d -> p k d", p=P)).then_inc(wqk_in, 16)
            load_xt(0)
            for m in range(MT):
                sp.dma_start(adj_sb[:, m, :], adj[m * P:(m + 1) * P, :]).then_inc(adj_in[m], 16)
                if m == 1:
                    sp.dma_start(wv_raw[:, :, :], wvT.rearrange("(k p) d -> p k d", p=P)).then_inc(wv_in, 16)

            def unit(u, k):
                if k % 2 == 0 and not (isinstance(u, int) and u == UNITS - 2):
                    if isinstance(u, int) and u == 0:
                        sp.wait_ge(xt_hi_done, PH)
                        sp.wait_ge(xt0_lo_done, PH)
                    else:
                        sp.wait_ge(xt_hi_done, u * (PH // 2) + PH)
                        sp.wait_ge(xt_lo_done, u * (PH // 2))
                    if isinstance(u, int):
                        load_xt(u // 2 + 1)
                    else:
                        sp.dma_start(xt_raw[:, :, :],
                                     xT_rows[bass.ds(u * (D // 2) + D, D), :].rearrange(
                                         "(k p) n -> p k n", p=P)).then_inc(xt_in, 16)
                if not (isinstance(u, int) and u < 2):
                    sp.wait_ge(normalised, u * NT - NT)
                    store(u - 2, k)
                    if k % 2 == 0:
                        sp.wait_ge(stored[0], u * 8)
                    else:
                        sp.wait_ge(stored[1], u * 8 - 8)
                load_x(u, k)

            run_units(sp, unit)
            sp.wait_ge(normalised, (UNITS - 1) * NT)
            store(UNITS - 2, 0)
            for n in range(NT):
                sp.wait_ge(normalised, (UNITS - 1) * NT + n + 1)
                r0 = (UNITS - 1) * HALF + n * P
                sp.dma_start(out_rows[r0:r0 + P, :], xo[1][:, n, :]).then_inc(stored[1], 16)
            sp.wait_ge(stored[0], 16 * B)
            sp.wait_ge(stored[1], 16 * (B - 1) + 16 * NT)

        @block.tensor
        def _(pe):
            def mm(o, l, r, start, stop):
                return nc.tensor.matmul(o, l, r, start=start, stop=stop)

            pe.wait_ge(wqk_in, 32)
            for dt in range(KT):
                for e in range(KT):
                    last = mm(g_ps[:, dt * D:(dt + 1) * D], wq_sb[:, e, dt * P:(dt + 1) * P], wk_sb[:, e, :],
                              e == 0, e == KT - 1)
            last.then_inc(g_done, 1)

            def project_y(u, k):
                xh, xl = xt_hi[k // 2], xt_lo[k // 2]
                if isinstance(u, int) and u == 0:
                    pe.wait_ge(g_hi_done, 1)
                    pe.wait_ge(g_lo_done, 1)
                for i in range(PH):
                    if isinstance(u, int) and u == 0:
                        if i % KT == 0:
                            pe.wait_ge(xt_hi_done, i + KT)
                            pe.wait_ge(xt0_lo_done, i + KT)
                    else:
                        if i == 0:
                            pe.wait_ge(xt_hi_done, u * (PH // 2) + PH)
                            pe.wait_ge(xt_lo_done, u * (PH // 2))
                        free_rel(u - 1, MT - PH + i)
                    c, e = i // KT, i % KT
                    n_ = slice(c * HALF, (c + 1) * HALF)
                    e_ = slice(e * P, (e + 1) * P)
                    for d in range(KT):
                        mm(ring[i][:, :], g_hi[:, d, e_], xh[:, d, n_], d == 0, False)
                        mm(ring[i][:, :], g_hi[:, d, e_], xl[:, d, n_], False, False)
                        last = mm(ring[i][:, :], g_lo[:, d, e_], xh[:, d, n_], False, d == KT - 1)
                    last.then_inc(tile_full, 1)

            def project_v(u, k):
                xh, xl = xt_hi[k // 2], xt_lo[k // 2]
                if isinstance(u, int) and u == 1:
                    pe.wait_ge(wv_hi_done, 1)
                    pe.wait_ge(wv_lo_done, 1)
                for i in range(PH):
                    free_rel(u - 1, MT - PH + i)
                    for s in range(2):
                        m_ = slice((2 * i + s) * P, (2 * i + s + 1) * P)
                        o = ring[i][:, s * D:(s + 1) * D]
                        for d in range(KT):
                            mm(o, xh[:, d, m_], wv_hl[:, d, 0, :], d == 0, False)
                            mm(o, xh[:, d, m_], wv_hl[:, d, 1, :], False, False)
                            last = mm(o, xl[:, d, m_], wv_hl[:, d, 0, :], False, d == KT - 1)
                    last.then_inc(tile_full, 1)

            def free_rel(u, j):
                pe.wait_ge(lo_done, u * UT + (PH + j + 1))

            def scores(u, k, j):
                if j == 0:
                    pe.wait_ge(lo_done, u * UT + KT)
                elif j < PH:
                    pe.wait_ge(lo_done, u * UT + (j + 1))
                else:
                    free_rel(u, j - PH)
                xh, xl = xt_hi[k // 2], xt_lo[k // 2]
                n_ = slice((k % 2) * HALF, (k % 2 + 1) * HALF)
                m_ = slice(j * P, (j + 1) * P)
                o = ring[j % RING][:, :]
                for d in range(KT):
                    mm(o, xh[:, d, m_], y_hi[:, d, n_], d == 0, False)
                    mm(o, xh[:, d, m_], y_lo[:, d, n_], False, False)
                    last = mm(o, xl[:, d, m_], y_hi[:, d, n_], False, d == KT - 1)
                last.then_inc(tile_full, 1)

            def rel_v(u, k, j):
                n, c, h = j // 2, j % 2, (k - 1) % 2
                if j == 0:
                    pe.wait_ge(lo_done, u * UT + PH if k % 2 else u * UT)
                if c == 0 and not (isinstance(u, int) and u == 1 and n < 2):
                    pe.wait_ge(pv_free, u * NT + (n - NT - 1))
                o = pv[n % 2]
                n_ = slice(n * P, (n + 1) * P)
                for m in range(c * MT // 2, (c + 1) * MT // 2):
                    hi = (o[:, :], rel_hi[h][:, m, n_], v_hl[:, m, :, :].rearrange("p a d -> p (a d)"))
                    lo = (o[:, 0:D], rel_lo[h][:, m, n_], v_hl[:, m, 0, :])
                    if m < MT - 1:
                        mm(*hi, m == 0, False)
                        mm(*lo, False, False)
                    else:
                        mm(*lo, False, False)
                        mm(*hi, False, True).then_inc(pv_full, 1)

            def norms(u, k):
                h = (k - 1) % 2
                pe.wait_ge(added, u * ADDS)
                if isinstance(u, int) and u == 1:
                    pe.wait_ge(ones_done, 1)
                if not (isinstance(u, int) and u < 2):
                    pe.wait_ge(normsq_done, u - 1)
                for n in range(NT):
                    last = mm(norm_ps[:, n:n + 1], sqsum[h][:, n * P:(n + 1) * P], ones[:, :],
                              True, True)
                last.then_inc(norm_full, 1)

            def unit(u, k):
                (project_v if k % 2 else project_y)(u, k)
                first = isinstance(u, int) and u == 0
                for j in range(MT):
                    scores(u, k, j)
                    if first or j == 0:
                        continue
                    if j == 2:
                        norms(u, k)
                    rel_v(u, k, j - 1)
                if not first:
                    rel_v(u, k, MT - 1)

            run_units(pe, unit)
            for j in range(MT):
                if j == 1:
                    norms(UNITS, 0)
                rel_v(UNITS, 0, j)

        @block.scalar
        def _(act):
            def to_hi(dst, src):
                return nc.scalar.activation(dst, src, ACT.Copy)

            act.wait_ge(xt_in, 16)
            for i in range(PH):
                to_hi(piece(xt_hi[0], i), piece(xt_raw, i)).then_inc(xt_hi_done, 1)
            act.wait_ge(g_done, 1)
            to_hi(g_hi[:, :, :].rearrange("p k d -> p (k d)"), g_ps[:, :]).then_inc(g_hi_done, 1)
            act.wait_ge(wv_in, 16)
            to_hi(wv_hl[:, :, 0, :], wv_raw[:, :, :]).then_inc(wv_hi_done, 1)

            def normalise(u, k, n, count):
                act.wait_ge(shift_done, count)
                t = xo[k % 2][:, n, :]
                nc.scalar.activation(t, t, ACT.Identity, bias=shift[k % 2][:, n:n + 1],
                                     scale=rstd[k % 2][:, n:n + 1]).then_inc(normalised, 1)

            def unit(u, k):
                h = k % 2
                for i in range(PH):
                    act.wait_ge(tile_full, u * UT + (i + 1))
                    if h:
                        dst = v_hl[:, 2 * i:2 * i + 2, 0, :]
                        src = ring[i][:, :].rearrange("p (s d) -> p s d", s=2)
                    else:
                        dst, src = piece(y_hi, i), ring[i][:, :]
                    to_hi(dst, src).then_inc(hi_done, 1)
                for j in range(MT):
                    act.wait_ge(masked, u * MT + (j + 1))
                    to_hi(rel_hi[h][:, j, :], ring[j % RING][:, :]).then_inc(hi_done, 1)
                    if j == 0:
                        dst = sqsum[h]
                        if not (isinstance(u, int) and u < 2):
                            act.wait_ge(norm_full, u - 1)
                    else:
                        g = (ADDS * h + j - 1) % 2
                        dst = sq[g]
                        if not (isinstance(u, int) and u == 0 and j < 3):
                            act.wait_ge(added, u * ADDS + (j - 2))
                    nc.scalar.activation(dst[:, :], ring[j % RING][:, :], ACT.Square).then_inc(squared, 1)
                    if j >= 5 and not (isinstance(u, int) and u < 2):
                        for n in ((0,), (1,), (2, 3))[j - 5]:
                            normalise(u - 2, k, n, u - 1)
                    if h and j % 2 == 0 and not (isinstance(u, int) and u == UNITS - 1):
                        i = j // 2
                        if i == 0:
                            act.wait_ge(xt_in, u * 8 + 24)
                        to_hi(piece(xt_hi[(k // 2 + 1) % 2], i), piece(xt_raw, i)).then_inc(xt_hi_done, 1)

            run_units(act, unit)
            for n in range(NT):
                normalise(UNITS - 2, 0, n, UNITS - 1)
            for n in range(NT):
                normalise(UNITS - 1, 1, n, UNITS + n)

        @block.gpsimd
        def _(pool):
            nc.gpsimd.memset(ones[:, :], 1.0).then_inc(ones_done, 1)
            nc.gpsimd.memset(minus_half[:, :], -0.5).then_inc(ones_done, 1)
            pool.wait_ge(ones_done, 2)

            def inverse_norm(w, kw):
                h = kw % 2
                pool.wait_ge(normsq_done, w + 1)
                nc.gpsimd.tensor_tensor(rnorm[h][:, :], normsq[h][:, :], minus_half[:, :],
                                        ALU.pow).then_inc(rnorm_done, 1)

            def inverse_deviation(w, kw, n0, n1, count):
                pool.wait_ge(var_done, count)
                nc.gpsimd.tensor_tensor(rstd[kw % 2][:, n0:n1], var_eps[:, n0:n1], minus_half[:, n0:n1],
                                        ALU.pow).then_inc(rstd_done, 1)

            def unit(u, k):
                h = k % 2
                for j in range(1, MT):
                    pool.wait_ge(squared, u * MT + (j + 1))
                    if not (isinstance(u, int) and u == 0 and j == 1):
                        pool.wait_ge(added, u * ADDS + (j - 1))
                    g = (ADDS * h + j - 1) % 2
                    nc.gpsimd.tensor_tensor(sqsum[h][:, :], sqsum[h][:, :], sq[g][:, :], ALU.add).then_inc(added, 1)
                    if j == 3 and not (isinstance(u, int) and u == 0):
                        inverse_norm(u - 1, (k - 1) % BODY)
                        if not (isinstance(u, int) and u == 1):
                            inverse_deviation(u - 2, (k - 2) % BODY, 0, NT, u - 1)
                    if h and j % 2 == 1 and not (isinstance(u, int) and u == UNITS - 1):
                        i = j // 2
                        nb = (k // 2 + 1) % 2
                        pool.wait_ge(xt_hi_done, u * 2 + (PH - 2 + i + 1))
                        nc.gpsimd.tensor_tensor(piece(xt_lo[nb], i), piece(xt_raw, i),
                                                piece(xt_hi[nb], i).bitcast(F32),
                                                ALU.subtract).then_inc(xt_lo_done, 1)

            run_units(pool, unit)
            inverse_deviation(UNITS - 2, 0, 0, NT, UNITS - 1)
            inverse_norm(UNITS - 1, 1)
            for n in range(NT):
                inverse_deviation(UNITS - 1, 1, n, n + 1, UNITS + n)

        @block.vector
        def _(dve):
            def to_lo(dst, src, hi):
                return nc.vector.tensor_tensor(dst, src, hi.bitcast(F32), ALU.subtract)

            for i in range(PH):
                dve.wait_ge(xt_hi_done, i + 1)
                to_lo(piece(xt_lo[0], i), piece(xt_raw, i), piece(xt_hi[0], i)).then_inc(xt0_lo_done, 1)
            dve.wait_ge(g_hi_done, 1)
            to_lo(g_lo[:, :, :].rearrange("p k d -> p (k d)"), g_ps[:, :],
                  g_hi[:, :, :].rearrange("p k d -> p (k d)")).then_inc(g_lo_done, 1)
            dve.wait_ge(wv_hi_done, 1)
            to_lo(wv_hl[:, :, 1, :], wv_raw[:, :, :], wv_hl[:, :, 0, :]).then_inc(wv_lo_done, 1)

            def mask(u, k, j):
                if isinstance(u, int) and u == 0:
                    dve.wait_ge(adj_in[j], 16)
                dve.wait_ge(tile_full, u * UT + (PH + j + 1))
                t = ring[j % RING][:, :]
                nc.vector.tensor_tensor(t, t, adj_sb[:, j, (k % 2) * HALF:(k % 2 + 1) * HALF],
                                        ALU.mult).then_inc(masked, 1)

            def phase_lo(u, k, i):
                dve.wait_ge(hi_done, u * UT + (i + 1))
                if k % 2:
                    v = v_hl[:, 2 * i:2 * i + 2, :, :]
                    ins = to_lo(v[:, :, 1, :], ring[i][:, :].rearrange("p (s d) -> p s d", s=2), v[:, :, 0, :])
                else:
                    ins = to_lo(piece(y_lo, i), ring[i][:, :], piece(y_hi, i))
                ins.then_inc(lo_done, 1)

            def rel_split(u, k, j):
                dve.wait_ge(squared, u * MT + (j + 1))
                h = k % 2
                to_lo(rel_lo[h][:, j, :], ring[j % RING][:, :], rel_hi[h][:, j, :]).then_inc(lo_done, 1)

            def norm_squares(w, kw):
                h = kw % 2
                dve.wait_ge(norm_full, w + 1)
                nc.vector.tensor_copy(normsq[h][:, :], norm_ps[:, 0:NT]).then_inc(normsq_done, 1)

            def add_x(w, kw, n):
                h = kw % 2
                dve.wait_ge(pv_full, w * NT + (n + 1))
                if n == 0:
                    dve.wait_ge(rnorm_done, w + 1)
                    dve.wait_ge(x_in[h], w * 8 + (8 if h else 16))
                t = xo[h][:, n, :]
                nc.vector.scalar_tensor_tensor(t, pv[n % 2][:, 0:D], rnorm[h][:, n:n + 1], t,
                                               ALU.mult, ALU.add).then_inc(x_added, 1)

            def add_cross(w, kw, n):
                h = kw % 2
                dve.wait_ge(x_added, w * NT + (n + 1))
                t = xo[h][:, n, :]
                nc.vector.scalar_tensor_tensor(t, pv[n % 2][:, D:2 * D], rnorm[h][:, n:n + 1], t,
                                               ALU.mult, ALU.add).then_inc(pv_free, 1)

            def tile_stats(w, kw, n):
                dve.wait_ge(pv_free, w * NT + (n + 1))
                nc.vector.bn_stats(stats[n % 2][:, :], xo[kw % 2][:, n, :]).then_inc(stats_done, 1)

            def tile_aggr(w, kw, n):
                nc.vector.bn_aggr(meanvar[:, n, :], stats[n % 2][:, :]).then_inc(aggr_done, 1)

            def variance(w, n0, n1):
                dve.wait_ge(aggr_done, w * NT + n1)
                nc.vector.tensor_scalar_add(var_eps[:, n0:n1], meanvar[:, n0:n1, 1], EPS).then_inc(var_done, 1)

            def shift_of(w, kw, n0, n1, count):
                h = kw % 2
                dve.wait_ge(rstd_done, count)
                nc.vector.scalar_tensor_tensor(shift[h][:, n0:n1], meanvar[:, n0:n1, 0], -1.0, rstd[h][:, n0:n1],
                                               ALU.mult, ALU.mult).then_inc(shift_done, 1)

            def unit(u, k):
                one = isinstance(u, int) and u == 0
                two = isinstance(u, int) and u == 1
                p, kp = u - 1, (k - 1) % BODY
                q, kq = u - 2, (k - 2) % BODY
                has_p, has_q = not one, not (one or two)
                for i in range(PH):
                    phase_lo(u, k, i)
                    if has_q:
                        if i == 0:
                            add_x(q, kq, 2)
                        elif i == 1:
                            add_cross(q, kq, 2)
                        elif i == 2:
                            tile_stats(q, kq, 2)
                if has_q:
                    dve.wait_ge(stats_done, q * NT + 3)
                mask(u, k, 0)
                if has_q:
                    tile_aggr(q, kq, 2)
                    add_x(q, kq, 3)
                mask(u, k, 1)
                if has_q:
                    add_cross(q, kq, 3)
                rel_split(u, k, 0)
                mask(u, k, 2)
                if has_q:
                    tile_stats(q, kq, 3)
                    dve.wait_ge(stats_done, q * NT + 4)
                rel_split(u, k, 1)
                if has_q:
                    tile_aggr(q, kq, 3)
                mask(u, k, 3)
                if has_p:
                    norm_squares(p, kp)
                if has_q:
                    variance(q, 0, NT)
                rel_split(u, k, 2)
                for j in range(4, MT):
                    n = (j - 4) // 2
                    mask(u, k, j)
                    if has_p:
                        if j % 2 == 0:
                            add_x(p, kp, n)
                        else:
                            tile_stats(p, kp, n)
                            dve.wait_ge(stats_done, p * NT + (n + 1))
                    rel_split(u, k, j - 1)
                    if has_q and j == 4:
                        shift_of(q, kq, 0, NT, q + 1)
                    if has_p:
                        if j % 2 == 0:
                            add_cross(p, kp, n)
                        else:
                            tile_aggr(p, kp, n)
                rel_split(u, k, MT - 1)

            run_units(dve, unit)
            q, kq = UNITS - 2, (UNITS - 2) % BODY
            for n in (2, 3):
                add_x(q, kq, n)
                add_cross(q, kq, n)
                tile_stats(q, kq, n)
                dve.wait_ge(stats_done, q * NT + n + 1)
                tile_aggr(q, kq, n)
            variance(q, 0, NT)
            shift_of(q, kq, 0, NT, q + 1)
            p, kp = UNITS - 1, (UNITS - 1) % BODY
            norm_squares(p, kp)
            for n in range(NT):
                add_x(p, kp, n)
                add_cross(p, kp, n)
                tile_stats(p, kp, n)
                dve.wait_ge(stats_done, p * NT + n + 1)
                tile_aggr(p, kp, n)
                variance(p, n, n + 1)
                shift_of(p, kp, n, n + 1, p + n + 1)


def kernel(x, adj, L0_gnn_Wq, L0_gnn_Wk, L0_gnn_Wv):
    import concourse.bacc as bacc
    from concourse.bass_utils import run_bass_kernel_spmd

    nc = bacc.Bacc("TRN2", target_bir_lowering=False, num_devices=1)
    x = np.ascontiguousarray(x)
    arrays = {
        "x": x,
        "xT": np.ascontiguousarray(x.transpose(0, 2, 1)),
        "adj": np.ascontiguousarray(adj),
        "wq": np.ascontiguousarray(L0_gnn_Wq),
        "wk": np.ascontiguousarray(L0_gnn_Wk),
        "wvT": np.ascontiguousarray(np.asarray(L0_gnn_Wv).T),
    }
    args = [nc.dram_tensor(name, a.shape, F32, kind="ExternalInput").ap() for name, a in arrays.items()]
    out = nc.dram_tensor("out", x.shape, F32, kind="ExternalOutput").ap()
    build(nc, *args, out)
    r = run_bass_kernel_spmd(nc, [arrays], core_ids=[0])
    return r.results[0]["out"]
```

```python
import numpy as np
import concourse.bass as bass
from concourse import mybir
from contextlib import ExitStack

F32 = mybir.dt.float32
F32R = mybir.dt.float32r
ALU = mybir.AluOpType
ACT = mybir.ActivationFunctionType

B, N, D = 8, 1024, 256
P = 128
KT = D // P
MT = N // P
HALF = N // 2
NT = HALF // P
UNITS = 2 * B
RING = 4
PH = 4
WARM = (6, 7)
UT = PH + MT
ADDS = MT - 1
EPS = 1e-5
PEEL = 2
BODY = 4
TRIPS = (UNITS - PEEL - 2) // BODY
assert PEEL + BODY * TRIPS == UNITS - 2 and UT % RING == 0


def run_units(eng, unit):
    for u in range(PEEL):
        unit(u, u)
    with eng.Fori(0, TRIPS) as i:
        for s in range(BODY):
            unit(i * BODY + (PEEL + s), (PEEL + s) % BODY)
    for u in range(UNITS - 2, UNITS):
        unit(u, u % BODY)


def build(nc, x, xT, adj, wq, wk, wvT, out):
    ctx = ExitStack()
    with ctx:
        def sb(name, shape, dt=F32):
            return ctx.enter_context(nc.sbuf_tensor(name, shape, dt))

        def bank(name):
            return ctx.enter_context(nc.psum_tensor(name, [P, 512], F32))

        def sem(name):
            return ctx.enter_context(nc.semaphore(name))

        adj_sb = sb("adj_sb", [P, MT, N])
        xt_raw = sb("xt_raw", [P, KT, N])
        xt_hi = [sb(f"xt_hi{i}", [P, KT, N], F32R) for i in range(2)]
        xt_lo = [sb(f"xt_lo{i}", [P, KT, N], F32R) for i in range(2)]
        y_hi = sb("y_hi", [P, KT, N], F32R)
        y_lo = sb("y_lo", [P, KT, N], F32R)
        v_hl = sb("v_hl", [P, MT, 2, D], F32R)
        rel_hi = [sb(f"rel_hi{h}", [P, MT, HALF], F32R) for h in range(2)]
        rel_lo = [sb(f"rel_lo{h}", [P, MT, HALF], F32R) for h in range(2)]
        sq = [sb(f"sq{i}", [P, HALF]) for i in range(2)]
        sqsum = sb("sqsum", [P, HALF])
        sqsum_hi = sb("sqsum_hi", [P, HALF], F32R)
        sqsum_lo = sb("sqsum_lo", [P, HALF], F32R)
        xo = [sb(f"xo{h}", [P, NT, D]) for h in range(2)]
        wq_sb = sb("wq_sb", [P, KT, D])
        wk_sb = sb("wk_sb", [P, KT, D])
        wv_raw = sb("wv_raw", [P, KT, D])
        wv_hl = sb("wv_hl", [P, KT, 2, D], F32R)
        g_hi = sb("g_hi", [P, KT, D], F32R)
        g_lo = sb("g_lo", [P, KT, D], F32R)
        ones_hi = sb("ones_hi", [P, P], F32R)
        diagonal = sb("diagonal", [P, NT, P])
        own_sum = sb("own_sum", [P, NT, P])
        minus_half = sb("minus_half", [P, NT])
        normsq = [sb(f"normsq{h}", [P, NT]) for h in range(2)]
        rnorm = [sb(f"rnorm{h}", [P, NT]) for h in range(2)]
        stats = [sb(f"stats{i}", [P, 6]) for i in range(2)]
        meanvar = [sb(f"meanvar{h}", [P, NT, 2]) for h in range(2)]
        var_eps = sb("var_eps", [P, NT])
        rstd = [sb(f"rstd{h}", [P, NT]) for h in range(2)]

        ring = [bank(f"ring{i}") for i in range(RING)]
        pv_a, pv_b, pv_c = (bank(f"pv_{i}") for i in "abc")
        pv = [pv_a, pv_b, pv_c, pv_b]
        g_norm = bank("g_norm")

        wqk_in = sem("wqk_in")
        wv_in = sem("wv_in")
        adj_in = [sem(f"adj_in{m}") for m in range(MT)]
        xt0_in = [sem(f"xt0_in{c}") for c in range(2)]
        xt_in = sem("xt_in")
        x_in = [sem(f"x_in{h}") for h in range(2)]
        stored = [sem(f"stored{h}") for h in range(2)]
        g_done = sem("g_done")
        g_hi_done = sem("g_hi_done")
        g_lo_done = sem("g_lo_done")
        wv_hi_done = sem("wv_hi_done")
        wv_lo_done = sem("wv_lo_done")
        ones_hi_done = sem("ones_hi_done")
        minus_half_done = sem("minus_half_done")
        diagonal_done = sem("diagonal_done")
        zeros_done = sem("zeros_done")
        xt_hi_done = sem("xt_hi_done")
        xt0_lo_done = sem("xt0_lo_done")
        xt_lo_done = sem("xt_lo_done")
        tile_full = sem("tile_full")
        masked = sem("masked")
        hi_done = sem("hi_done")
        lo_done = sem("lo_done")
        squared = sem("squared")
        added = sem("added")
        sum_hi_done = sem("sum_hi_done")
        sum_lo_done = sem("sum_lo_done")
        norm_full = sem("norm_full")
        diagonal_kept = sem("diagonal_kept")
        normsq_done = sem("normsq_done")
        rnorm_done = sem("rnorm_done")
        pv_full = sem("pv_full")
        x_added = sem("x_added")
        pv_free = sem("pv_free")
        stats_done = sem("stats_done")
        aggr_done = sem("aggr_done")
        var_done = sem("var_done")
        rstd_done = sem("rstd_done")
        normalised = sem("normalised")

        def batch_rows(t, u, k):
            return t[bass.ds(u * HALF, HALF), :].rearrange("(t p) d -> p t d", p=P)

        x_rows = x.rearrange("b n d -> (b n) d")
        out_rows = out.rearrange("b n d -> (b n) d")
        xT_rows = xT.rearrange("b d n -> (b d) n")

        def half_of(t, h):
            return slice(h * HALF, (h + 1) * HALF)

        def piece(t, i):
            return t[:, i % KT, (i // KT) * HALF:(i // KT + 1) * HALF]

        block = ctx.enter_context(nc.Block())

        @block.sync
        def _(sp):
            def load_x(u, k):
                sp.dma_start(xo[k % 2][:, :, :], batch_rows(x_rows, u, k)).then_inc(x_in[k % 2], 16)

            def store(u, k):
                sp.dma_start(batch_rows(out_rows, u, k), xo[k % 2][:, :, :]).then_inc(stored[k % 2], 16)

            sp.dma_start(wq_sb[:, :, :], wq.rearrange("(k p) d -> p k d", p=P)).then_inc(wqk_in, 16)
            sp.dma_start(wk_sb[:, :, :], wk.rearrange("(k p) d -> p k d", p=P)).then_inc(wqk_in, 16)
            for c in range(2):
                n_ = slice(c * HALF, (c + 1) * HALF)
                sp.dma_start(xt_raw[:, :, n_], xT[0, :, n_].rearrange("(k p) n -> p k n", p=P)).then_inc(xt0_in[c], 16)
            sp.dma_start(wv_raw[:, :, :], wvT.rearrange("(k p) d -> p k d", p=P)).then_inc(wv_in, 16)
            for m in range(MT):
                sp.dma_start(adj_sb[:, m, :], adj[m * P:(m + 1) * P, :]).then_inc(adj_in[m], 16)

            def unit(u, k):
                if k % 2 == 0 and not (isinstance(u, int) and u == UNITS - 2):
                    if isinstance(u, int) and u == 0:
                        sp.wait_ge(xt_hi_done, PH)
                        sp.wait_ge(xt0_lo_done, PH)
                    else:
                        sp.wait_ge(xt_hi_done, u * (PH // 2) + PH)
                        sp.wait_ge(xt_lo_done, u * (PH // 2))
                    sp.dma_start(xt_raw[:, :, :], xT_rows[bass.ds(u * (D // 2) + D, D), :].rearrange(
                        "(k p) n -> p k n", p=P)).then_inc(xt_in, 16)
                if not (isinstance(u, int) and u < 2):
                    sp.wait_ge(normalised, u * NT - NT)
                    store(u - 2, k)
                    if k % 2 == 0:
                        sp.wait_ge(stored[0], u * 8)
                    else:
                        sp.wait_ge(stored[1], u * 8 - 8)
                load_x(u, k)

            run_units(sp, unit)
            sp.wait_ge(normalised, (UNITS - 1) * NT)
            store(UNITS - 2, 0)
            for n in range(NT):
                sp.wait_ge(normalised, (UNITS - 1) * NT + n + 1)
                r0 = (UNITS - 1) * HALF + n * P
                sp.dma_start(out_rows[r0:r0 + P, :], xo[1][:, n, :]).then_inc(stored[1], 16)
            sp.wait_ge(stored[0], 16 * B)
            sp.wait_ge(stored[1], 16 * (B - 1) + 16 * NT)

        @block.tensor
        def _(pe):
            def mm(o, l, r, start, stop):
                return nc.tensor.matmul(o, l, r, start=start, stop=stop)

            def keep_warm(count):
                for _ in range(count):
                    mm(ring[RING - 1][:, 0:P], sq[0][:, 0:P], sq[0][:, 0:P], True, True)

            pe.wait_ge(zeros_done, 1)
            keep_warm(WARM[0])
            pe.wait_ge(wqk_in, 32)
            for dt in range(KT):
                for e in range(KT):
                    last = mm(g_norm[:, dt * D:(dt + 1) * D], wq_sb[:, e, dt * P:(dt + 1) * P], wk_sb[:, e, :],
                              e == 0, e == KT - 1)
            last.then_inc(g_done, 1)
            keep_warm(WARM[1])

            def project_y(u, k):
                xh, xl = xt_hi[k // 2], xt_lo[k // 2]
                if isinstance(u, int) and u == 0:
                    pe.wait_ge(g_hi_done, 1)
                    pe.wait_ge(g_lo_done, 1)
                for i in range(PH):
                    if isinstance(u, int) and u == 0:
                        if i % KT == 0:
                            pe.wait_ge(xt_hi_done, i + KT)
                            pe.wait_ge(xt0_lo_done, i + KT)
                    else:
                        if i == 0:
                            pe.wait_ge(xt_hi_done, u * (PH // 2) + PH)
                            pe.wait_ge(xt_lo_done, u * (PH // 2))
                        free_rel(u - 1, MT - PH + i)
                    c, e = i // KT, i % KT
                    n_ = slice(c * HALF, (c + 1) * HALF)
                    e_ = slice(e * P, (e + 1) * P)
                    for d in range(KT):
                        mm(ring[i][:, :], g_hi[:, d, e_], xh[:, d, n_], d == 0, False)
                        mm(ring[i][:, :], g_hi[:, d, e_], xl[:, d, n_], False, False)
                        last = mm(ring[i][:, :], g_lo[:, d, e_], xh[:, d, n_], False, d == KT - 1)
                    last.then_inc(tile_full, 1)

            def project_v(u, k):
                xh, xl = xt_hi[k // 2], xt_lo[k // 2]
                if isinstance(u, int) and u == 1:
                    pe.wait_ge(wv_hi_done, 1)
                    pe.wait_ge(wv_lo_done, 1)
                for i in range(PH):
                    free_rel(u - 1, MT - PH + i)
                    for s in range(2):
                        m_ = slice((2 * i + s) * P, (2 * i + s + 1) * P)
                        o = ring[i][:, s * D:(s + 1) * D]
                        for d in range(KT):
                            mm(o, xh[:, d, m_], wv_hl[:, d, 0, :], d == 0, False)
                            mm(o, xh[:, d, m_], wv_hl[:, d, 1, :], False, False)
                            last = mm(o, xl[:, d, m_], wv_hl[:, d, 0, :], False, d == KT - 1)
                    last.then_inc(tile_full, 1)

            def free_rel(u, j):
                pe.wait_ge(lo_done, u * UT + (PH + j + 1))

            def norms(u, k):
                pe.wait_ge(sum_lo_done, u)
                if isinstance(u, int) and u == 1:
                    pe.wait_ge(ones_hi_done, 1)
                if not (isinstance(u, int) and u < 2):
                    pe.wait_ge(diagonal_kept, u - 1)
                mm(g_norm[:, :], ones_hi[:, :], sqsum_hi[:, :], True, False)
                mm(g_norm[:, :], ones_hi[:, :], sqsum_lo[:, :], False, True).then_inc(norm_full, 1)

            def scores(u, k, j):
                if j == 0:
                    pe.wait_ge(lo_done, u * UT + KT)
                elif j < PH:
                    pe.wait_ge(lo_done, u * UT + (j + 1))
                else:
                    free_rel(u, j - PH)
                xh, xl = xt_hi[k // 2], xt_lo[k // 2]
                n_ = slice((k % 2) * HALF, (k % 2 + 1) * HALF)
                m_ = slice(j * P, (j + 1) * P)
                o = ring[j % RING][:, :]
                for d in range(KT):
                    mm(o, xh[:, d, m_], y_hi[:, d, n_], d == 0, False)
                    mm(o, xh[:, d, m_], y_lo[:, d, n_], False, False)
                    last = mm(o, xl[:, d, m_], y_hi[:, d, n_], False, d == KT - 1)
                last.then_inc(tile_full, 1)

            def rel_v(u, k, j):
                n, c, h = j // 2, j % 2, (k - 1) % 2
                last_unit = isinstance(u, int) and u == UNITS
                o = (ring if last_unit else pv)[n]
                if j == 0:
                    pe.wait_ge(lo_done, u * UT + PH if k % 2 else u * UT)
                if last_unit:
                    pass
                elif c == 0 and n == 3:
                    pe.wait_ge(pv_free, u * NT - NT + 2)
                elif c == 0 and not (isinstance(u, int) and u == 1):
                    pe.wait_ge(pv_free, u * NT - 2 * NT + (1, 4, 3)[n])
                n_ = slice(n * P, (n + 1) * P)
                for m in range(c * MT // 2, (c + 1) * MT // 2):
                    hi = (o[:, :], rel_hi[h][:, m, n_], v_hl[:, m, :, :].rearrange("p a d -> p (a d)"))
                    lo = (o[:, 0:D], rel_lo[h][:, m, n_], v_hl[:, m, 0, :])
                    if m < MT - 1:
                        mm(*hi, m == 0, False)
                        mm(*lo, False, False)
                    else:
                        mm(*lo, False, False)
                        mm(*hi, False, True).then_inc(pv_full, 1)

            def unit(u, k):
                (project_v if k % 2 else project_y)(u, k)
                first = isinstance(u, int) and u == 0
                for j in range(MT):
                    scores(u, k, j)
                    if j == 1 and not first:
                        norms(u, k)
                    if first or j == 0:
                        continue
                    rel_v(u, k, j - 1)
                if not first:
                    rel_v(u, k, MT - 1)

            run_units(pe, unit)
            for j in range(MT):
                if j == 2:
                    norms(UNITS, 0)
                rel_v(UNITS, 0, j)

        @block.scalar
        def _(act):
            def to_hi(dst, src):
                return nc.scalar.activation(dst, src, ACT.Copy)

            for i in range(PH):
                if i == KT:
                    act.wait_ge(g_done, 1)
                    to_hi(g_hi[:, :, :].rearrange("p k d -> p (k d)"), g_norm[:, :]).then_inc(g_hi_done, 1)
                if i % KT == 0:
                    act.wait_ge(xt0_in[i // KT], 16)
                to_hi(piece(xt_hi[0], i), piece(xt_raw, i)).then_inc(xt_hi_done, 1)
            act.wait_ge(wv_in, 16)
            to_hi(wv_hl[:, :, 0, :], wv_raw[:, :, :]).then_inc(wv_hi_done, 1)

            def split_sum(u):
                act.wait_ge(added, u * ADDS)
                if not (isinstance(u, int) and u < 2):
                    act.wait_ge(norm_full, u - 1)
                to_hi(sqsum_hi[:, :], sqsum[:, :]).then_inc(sum_hi_done, 1)

            def unit(u, k):
                h = k % 2
                for i in range(PH):
                    if i == 2 and not (isinstance(u, int) and u == 0):
                        split_sum(u)
                    act.wait_ge(tile_full, u * UT + (i + 1))
                    if h:
                        dst = v_hl[:, 2 * i:2 * i + 2, 0, :]
                        src = ring[i][:, :].rearrange("p (s d) -> p s d", s=2)
                    else:
                        dst, src = piece(y_hi, i), ring[i][:, :]
                    to_hi(dst, src).then_inc(hi_done, 1)
                for j in range(MT):
                    act.wait_ge(masked, u * MT + (j + 1))
                    to_hi(rel_hi[h][:, j, :], ring[j % RING][:, :]).then_inc(hi_done, 1)
                    if j == 0:
                        dst = sqsum
                        if not (isinstance(u, int) and u < 1):
                            act.wait_ge(sum_lo_done, u)
                    else:
                        g = (ADDS * h + j - 1) % 2
                        dst = sq[g]
                        if not (isinstance(u, int) and u == 0 and j < 3):
                            act.wait_ge(added, u * ADDS + (j - 2))
                    nc.scalar.activation(dst[:, :], ring[j % RING][:, :], ACT.Square).then_inc(squared, 1)
                    if h and j < PH and not (isinstance(u, int) and u == UNITS - 1):
                        i = j
                        if i == 0:
                            act.wait_ge(xt_in, u * 8 + 8)
                        to_hi(piece(xt_hi[(k // 2 + 1) % 2], i), piece(xt_raw, i)).then_inc(xt_hi_done, 1)

            run_units(act, unit)
            split_sum(UNITS)

        @block.gpsimd
        def _(pool):
            nc.gpsimd.memset(ones_hi[:, :].bitcast(F32), 1.0).then_inc(ones_hi_done, 1)
            nc.gpsimd.memset(minus_half[:, :], -0.5).then_inc(minus_half_done, 1)
            nc.gpsimd.memset(diagonal[:, :, :], 0.0).then_inc(diagonal_done, 1)
            pool.wait_ge(diagonal_done, 1)
            nc.gpsimd.affine_select(out=diagonal[:, :, :], in_=diagonal[:, :, :], compare_op=ALU.not_equal,
                                    fill=1.0, base=0, pattern=[[0, NT], [-1, P]],
                                    channel_multiplier=1).then_inc(diagonal_done, 1)
            pool.wait_ge(minus_half_done, 1)

            def inverse_norm(w, kw):
                h = kw % 2
                pool.wait_ge(normsq_done, w + 1)
                nc.gpsimd.tensor_tensor(rnorm[h][:, :], normsq[h][:, :], minus_half[:, :],
                                        ALU.pow).then_inc(rnorm_done, 1)

            def inverse_deviation(w, kw, n0, n1, count):
                pool.wait_ge(var_done, count)
                nc.gpsimd.tensor_tensor(rstd[kw % 2][:, n0:n1], var_eps[:, n0:n1], minus_half[:, n0:n1],
                                        ALU.pow).then_inc(rstd_done, 1)

            def split_sum(u):
                pool.wait_ge(sum_hi_done, u + 1)
                nc.gpsimd.tensor_tensor(sqsum_lo[:, :], sqsum[:, :], sqsum_hi[:, :].bitcast(F32),
                                        ALU.subtract).then_inc(sum_lo_done, 1)

            def unit(u, k):
                h = k % 2
                for j in range(1, MT):
                    pool.wait_ge(squared, u * MT + (j + 1))
                    if not (isinstance(u, int) and u == 0 and j == 1):
                        pool.wait_ge(added, u * ADDS + (j - 1))
                    g = (ADDS * h + j - 1) % 2
                    nc.gpsimd.tensor_tensor(sqsum[:, :], sqsum[:, :], sq[g][:, :], ALU.add).then_inc(added, 1)
                    if j == 3 and not (isinstance(u, int) and u == 0):
                        inverse_norm(u - 1, (k - 1) % BODY)
                    if j == 3 and not (isinstance(u, int) and u < 2):
                        inverse_deviation(u - 2, (k - 2) % BODY, 0, NT, u - 1)
                    if h and j in (1, 2, 4, 5) and not (isinstance(u, int) and u == UNITS - 1):
                        i = (1, 2, 4, 5).index(j)
                        nb = (k // 2 + 1) % 2
                        pool.wait_ge(xt_hi_done, u * 2 + (PH - 2 + i + 1))
                        nc.gpsimd.tensor_tensor(piece(xt_lo[nb], i), piece(xt_raw, i),
                                                piece(xt_hi[nb], i).bitcast(F32),
                                                ALU.subtract).then_inc(xt_lo_done, 1)
                split_sum(u)

            run_units(pool, unit)
            inverse_deviation(UNITS - 2, 0, 0, NT, UNITS - 1)
            inverse_norm(UNITS - 1, 1)
            for n in range(NT):
                inverse_deviation(UNITS - 1, 1, n, n + 1, UNITS + n)

        @block.vector
        def _(dve):
            def to_lo(dst, src, hi):
                return nc.vector.tensor_tensor(dst, src, hi.bitcast(F32), ALU.subtract)

            nc.vector.memset(sq[0][:, :], 0.0).then_inc(zeros_done, 1)
            nc.vector.memset(own_sum[:, :, :], 0.0).then_inc(zeros_done, 1)
            for i in range(PH):
                if i == KT:
                    dve.wait_ge(g_hi_done, 1)
                    to_lo(g_lo[:, :, :].rearrange("p k d -> p (k d)"), g_norm[:, :],
                          g_hi[:, :, :].rearrange("p k d -> p (k d)")).then_inc(g_lo_done, 1)
                dve.wait_ge(xt_hi_done, i + 1)
                to_lo(piece(xt_lo[0], i), piece(xt_raw, i), piece(xt_hi[0], i)).then_inc(xt0_lo_done, 1)
            dve.wait_ge(wv_hi_done, 1)
            to_lo(wv_hl[:, :, 1, :], wv_raw[:, :, :], wv_hl[:, :, 0, :]).then_inc(wv_lo_done, 1)

            def mask(u, k, j):
                if isinstance(u, int) and u == 0:
                    dve.wait_ge(adj_in[j], 16)
                dve.wait_ge(tile_full, u * UT + (PH + j + 1))
                t = ring[j % RING][:, :]
                nc.vector.tensor_tensor(t, t, adj_sb[:, j, (k % 2) * HALF:(k % 2 + 1) * HALF],
                                        ALU.mult).then_inc(masked, 1)

            def phase_lo(u, k, i):
                dve.wait_ge(hi_done, u * UT + (i + 1))
                if k % 2:
                    v = v_hl[:, 2 * i:2 * i + 2, :, :]
                    ins = to_lo(v[:, :, 1, :], ring[i][:, :].rearrange("p (s d) -> p s d", s=2), v[:, :, 0, :])
                else:
                    ins = to_lo(piece(y_lo, i), ring[i][:, :], piece(y_hi, i))
                ins.then_inc(lo_done, 1)

            def rel_split(u, k, j):
                dve.wait_ge(squared, u * MT + (j + 1))
                h = k % 2
                to_lo(rel_lo[h][:, j, :], ring[j % RING][:, :], rel_hi[h][:, j, :]).then_inc(lo_done, 1)

            def rel_v_bank(w, n):
                return (ring if isinstance(w, int) and w == UNITS - 1 else pv)[n]

            def keep_diagonal(w):
                t = g_norm[:, :].rearrange("p (t n) -> p t n", t=NT)
                nc.vector.copy_predicated(own_sum[:, :, :], diagonal[:, :, :].bitcast(mybir.dt.uint32),
                                          t).then_inc(diagonal_kept, 1)

            def norm_squares(w, kw):
                dve.wait_ge(diagonal_kept, w + 1)
                nc.vector.tensor_reduce(normsq[kw % 2][:, :], own_sum[:, :, :],
                                        mybir.AxisListType.X, ALU.add).then_inc(normsq_done, 1)

            def add_x(w, kw, n):
                h = kw % 2
                dve.wait_ge(pv_full, w * NT + (n + 1))
                if n == 0:
                    dve.wait_ge(rnorm_done, w + 1)
                    dve.wait_ge(x_in[h], w * 8 + (8 if h else 16))
                t = xo[h][:, n, :]
                nc.vector.scalar_tensor_tensor(t, rel_v_bank(w, n)[:, 0:D], rnorm[h][:, n:n + 1], t,
                                               ALU.mult, ALU.add).then_inc(x_added, 1)

            def add_cross(w, kw, n):
                h = kw % 2
                dve.wait_ge(x_added, w * NT + (n + 1))
                t = xo[h][:, n, :]
                nc.vector.scalar_tensor_tensor(t, rel_v_bank(w, n)[:, D:2 * D], rnorm[h][:, n:n + 1], t,
                                               ALU.mult, ALU.add).then_inc(pv_free, 1)

            def tile_stats(w, kw, n):
                dve.wait_ge(pv_free, w * NT + (n + 1))
                nc.vector.bn_stats(stats[n % 2][:, :], xo[kw % 2][:, n, :]).then_inc(stats_done, 1)

            def tile_aggr(w, kw, n):
                nc.vector.bn_aggr(meanvar[kw % 2][:, n, :], stats[n % 2][:, :]).then_inc(aggr_done, 1)

            def variance(w, kw, n0, n1):
                dve.wait_ge(aggr_done, w * NT + n1)
                nc.vector.tensor_scalar_add(var_eps[:, n0:n1], meanvar[kw % 2][:, n0:n1, 1],
                                            EPS).then_inc(var_done, 1)

            def normalise(w, kw, n, count):
                h = kw % 2
                dve.wait_ge(rstd_done, count)
                t = xo[h][:, n, :]
                nc.vector.tensor_scalar(t, t, meanvar[h][:, n, 0:1], rstd[h][:, n:n + 1],
                                        ALU.subtract, ALU.mult).then_inc(normalised, 1)

            def unit(u, k):
                one = isinstance(u, int) and u == 0
                two = isinstance(u, int) and u == 1
                p, kp = u - 1, (k - 1) % BODY
                q, kq = u - 2, (k - 2) % BODY
                has_p, has_q = not one, not (one or two)
                for i in range(PH):
                    phase_lo(u, k, i)
                    if has_q and i == 0:
                        add_x(q, kq, 2)
                    elif has_q and i == 1:
                        add_cross(q, kq, 2)
                    elif has_q and i == 2:
                        tile_stats(q, kq, 2)
                if has_q:
                    dve.wait_ge(stats_done, q * NT + 3)
                for j in range(MT):
                    if has_p and j == 3:
                        dve.wait_ge(norm_full, p + 1)
                    mask(u, k, j)
                    if has_q and j == 0:
                        tile_aggr(q, kq, 2)
                        add_x(q, kq, 3)
                    elif has_q and j == 1:
                        add_cross(q, kq, 3)
                    elif has_q and j == 2:
                        tile_stats(q, kq, 3)
                        dve.wait_ge(stats_done, q * NT + 4)
                    elif has_p and j == 3:
                        keep_diagonal(p)
                    elif has_p and j in (5, 6):
                        add_x(p, kp, j - 5)
                    elif has_p and j == 7:
                        tile_stats(p, kp, 0)
                    if j > 0:
                        rel_split(u, k, j - 1)
                    if has_q and j == 2:
                        tile_aggr(q, kq, 3)
                    elif has_p and j == 3:
                        norm_squares(p, kp)
                        if has_q:
                            variance(q, kq, 0, NT)
                    elif has_p and j in (5, 6):
                        add_cross(p, kp, j - 5)
                        if has_q and j == 6:
                            normalise(q, kq, 0, q + 1)
                    elif has_p and j == 7:
                        tile_stats(p, kp, 1)
                        if has_q:
                            normalise(q, kq, 1, q + 1)
                        dve.wait_ge(stats_done, p * NT + 2)
                rel_split(u, k, MT - 1)
                if has_p:
                    tile_aggr(p, kp, 0)
                    tile_aggr(p, kp, 1)
                if has_q:
                    normalise(q, kq, 2, q + 1)
                    normalise(q, kq, 3, q + 1)

            dve.wait_ge(zeros_done, 2)
            dve.wait_ge(diagonal_done, 2)
            run_units(dve, unit)
            q, kq = UNITS - 2, (UNITS - 2) % BODY
            for n in (2, 3):
                add_x(q, kq, n)
                add_cross(q, kq, n)
                tile_stats(q, kq, n)
                dve.wait_ge(stats_done, q * NT + n + 1)
                tile_aggr(q, kq, n)
            variance(q, kq, 0, NT)
            p, kp = UNITS - 1, (UNITS - 1) % BODY
            dve.wait_ge(norm_full, p + 1)
            keep_diagonal(p)
            norm_squares(p, kp)
            for n in range(NT):
                normalise(q, kq, n, q + 1)
            for n in range(NT):
                add_x(p, kp, n)
                add_cross(p, kp, n)
                tile_stats(p, kp, n)
                dve.wait_ge(stats_done, p * NT + n + 1)
                tile_aggr(p, kp, n)
                variance(p, kp, n, n + 1)
                normalise(p, kp, n, p + n + 1)


def kernel(x, adj, L0_gnn_Wq, L0_gnn_Wk, L0_gnn_Wv):
    import concourse.bacc as bacc
    from concourse.bass_utils import run_bass_kernel_spmd

    nc = bacc.Bacc("TRN2", target_bir_lowering=False, num_devices=1)
    x = np.ascontiguousarray(x)
    arrays = {
        "x": x,
        "xT": np.ascontiguousarray(x.transpose(0, 2, 1)),
        "adj": np.ascontiguousarray(adj),
        "wq": np.ascontiguousarray(L0_gnn_Wq),
        "wk": np.ascontiguousarray(L0_gnn_Wk),
        "wvT": np.ascontiguousarray(np.asarray(L0_gnn_Wv).T),
    }
    args = [nc.dram_tensor(name, a.shape, F32, kind="ExternalInput").ap() for name, a in arrays.items()]
    out = nc.dram_tensor("out", x.shape, F32, kind="ExternalOutput").ap()
    build(nc, *args, out)
    r = run_bass_kernel_spmd(nc, [arrays], core_ids=[0])
    return r.results[0]["out"]
```

```python
import numpy as np
import concourse.bass as bass
from concourse import mybir
from contextlib import ExitStack

F32 = mybir.dt.float32
F32R = mybir.dt.float32r
ALU = mybir.AluOpType
ACT = mybir.ActivationFunctionType

B, N, D = 8, 1024, 256
P = 128
KT = D // P
MT = N // P
HALF = N // 2
NT = HALF // P
UNITS = 2 * B
RING = 4
PH = 4
WARM = (6, 7)
UT = PH + MT
ADDS = MT - 1
EPS = 1e-5
PEEL = 2
BODY = 4
TRIPS = (UNITS - PEEL - 2) // BODY
assert PEEL + BODY * TRIPS == UNITS - 2 and UT % RING == 0


def at(u, n):
    return isinstance(u, int) and u == n


def before(u, n):
    return isinstance(u, int) and u < n


def run_units(eng, unit):
    for u in range(PEEL):
        unit(u, u)
    with eng.Fori(0, TRIPS) as i:
        for s in range(BODY):
            unit(i * BODY + (PEEL + s), (PEEL + s) % BODY)
    for u in range(UNITS - 2, UNITS):
        unit(u, u % BODY)


def build(nc, x, xT, adj, wq, wk, wvT, out):
    ctx = ExitStack()
    with ctx:
        def sb(name, shape, dt=F32):
            return ctx.enter_context(nc.sbuf_tensor(name, shape, dt))

        def bank(name):
            return ctx.enter_context(nc.psum_tensor(name, [P, 512], F32))

        def sem(name):
            return ctx.enter_context(nc.semaphore(name))

        adj_sb = sb("adj_sb", [P, MT, N])
        xt_raw = sb("xt_raw", [P, KT, N])
        xt_hi = [sb(f"xt_hi{i}", [P, KT, N], F32R) for i in range(2)]
        xt_lo = [sb(f"xt_lo{i}", [P, KT, N], F32R) for i in range(2)]
        y_hi = sb("y_hi", [P, KT, N], F32R)
        y_lo = sb("y_lo", [P, KT, N], F32R)
        v_hl = sb("v_hl", [P, MT, 2, D], F32R)
        rel_hi = [sb(f"rel_hi{h}", [P, MT, HALF], F32R) for h in range(2)]
        rel_lo = [sb(f"rel_lo{h}", [P, MT, HALF], F32R) for h in range(2)]
        sq = [sb(f"sq{i}", [P, HALF]) for i in range(2)]
        sqsum = sb("sqsum", [P, HALF])
        sqsum_hi = sb("sqsum_hi", [P, HALF], F32R)
        sqsum_lo = sb("sqsum_lo", [P, HALF], F32R)
        xo = [sb(f"xo{h}", [P, NT, D]) for h in range(2)]
        wq_sb = sb("wq_sb", [P, KT, D])
        wk_sb = sb("wk_sb", [P, KT, D])
        wv_raw = sb("wv_raw", [P, KT, D])
        wv_hl = sb("wv_hl", [P, KT, 2, D], F32R)
        g_hi = sb("g_hi", [P, KT, D], F32R)
        g_lo = sb("g_lo", [P, KT, D], F32R)
        ones_hi = sb("ones_hi", [P, P], F32R)
        diagonal = sb("diagonal", [P, NT, P])
        own_sum = sb("own_sum", [P, NT, P])
        minus_half = sb("minus_half", [P, NT])
        normsq = [sb(f"normsq{h}", [P, NT]) for h in range(2)]
        rnorm = [sb(f"rnorm{h}", [P, NT]) for h in range(2)]
        stats = [sb(f"stats{i}", [P, 6]) for i in range(2)]
        meanvar = [sb(f"meanvar{h}", [P, NT, 2]) for h in range(2)]
        var_eps = sb("var_eps", [P, NT])
        rstd = [sb(f"rstd{h}", [P, NT]) for h in range(2)]
        shift = [sb(f"shift{h}", [P, NT]) for h in range(2)]

        ring = [bank(f"ring{i}") for i in range(RING)]
        pv_a, pv_b, pv_c = (bank(f"pv_{i}") for i in "abc")
        pv = [pv_a, pv_b, pv_c, pv_b]
        last_pv = [pv_a, ring[0], ring[1], ring[2]]
        g_norm = bank("g_norm")

        wqk_in = sem("wqk_in")
        wv_in = sem("wv_in")
        adj_in = [sem(f"adj_in{m}") for m in range(MT)]
        xt0_in = [sem(f"xt0_in{c}") for c in range(2)]
        xt_in = sem("xt_in")
        x_in = [sem(f"x_in{h}") for h in range(2)]
        x_last_in = sem("x_last_in")
        stored = [sem(f"stored{h}") for h in range(2)]
        g_done = sem("g_done")
        g_hi_done = sem("g_hi_done")
        g_lo_done = sem("g_lo_done")
        wv_hi_done = sem("wv_hi_done")
        wv_lo_done = sem("wv_lo_done")
        ones_hi_done = sem("ones_hi_done")
        minus_half_done = sem("minus_half_done")
        diagonal_done = sem("diagonal_done")
        zeros_done = sem("zeros_done")
        xt_hi_done = sem("xt_hi_done")
        xt0_lo_done = sem("xt0_lo_done")
        xt_lo_done = sem("xt_lo_done")
        tile_full = sem("tile_full")
        masked = sem("masked")
        hi_done = sem("hi_done")
        lo_done = sem("lo_done")
        squared = sem("squared")
        added = sem("added")
        sum_hi_done = sem("sum_hi_done")
        sum_lo_done = sem("sum_lo_done")
        norm_full = sem("norm_full")
        diagonal_kept = sem("diagonal_kept")
        normsq_done = sem("normsq_done")
        rnorm_done = sem("rnorm_done")
        pv_full = sem("pv_full")
        x_added = sem("x_added")
        pv_free = sem("pv_free")
        stats_done = sem("stats_done")
        aggr_done = sem("aggr_done")
        var_done = sem("var_done")
        rstd_done = sem("rstd_done")
        shift_done = sem("shift_done")
        normalised = sem("normalised")
        last_normalised = sem("last_normalised")

        def unit_rows(t, u):
            return t[bass.ds(u * HALF, HALF), :].rearrange("(t p) d -> p t d", p=P)

        x_rows = x.rearrange("b n d -> (b n) d")
        out_rows = out.rearrange("b n d -> (b n) d")
        xT_rows = xT.rearrange("b d n -> (b d) n")

        def piece(t, i):
            return t[:, i % KT, (i // KT) * HALF:(i // KT + 1) * HALF]

        def xo_of(u, k):
            if at(u, UNITS - 1):
                return xt_raw[:, 0, :].rearrange("p (t d) -> p t d", t=NT)
            return xo[k % 2]

        block = ctx.enter_context(nc.Block())

        @block.sync
        def _(sp):
            def load_x(u, k):
                sp.dma_start(xo[k % 2][:, :, :], unit_rows(x_rows, u)).then_inc(x_in[k % 2], 16)

            def store(u, k):
                sp.dma_start(unit_rows(out_rows, u), xo[k % 2][:, :, :]).then_inc(stored[k % 2], 16)

            sp.dma_start(wq_sb[:, :, :], wq.rearrange("(k p) d -> p k d", p=P)).then_inc(wqk_in, 16)
            sp.dma_start(wk_sb[:, :, :], wk.rearrange("(k p) d -> p k d", p=P)).then_inc(wqk_in, 16)
            for c in range(2):
                n_ = slice(c * HALF, (c + 1) * HALF)
                sp.dma_start(xt_raw[:, :, n_], xT[0, :, n_].rearrange("(k p) n -> p k n", p=P)).then_inc(xt0_in[c], 16)
            sp.dma_start(wv_raw[:, :, :], wvT.rearrange("(k p) d -> p k d", p=P)).then_inc(wv_in, 16)
            for m in range(MT):
                sp.dma_start(adj_sb[:, m, :], adj[m * P:(m + 1) * P, :]).then_inc(adj_in[m], 16)

            def unit(u, k):
                if k % 2 == 0 and not at(u, UNITS - 2):
                    if at(u, 0):
                        sp.wait_ge(xt_hi_done, PH)
                        sp.wait_ge(xt0_lo_done, PH)
                    else:
                        sp.wait_ge(xt_hi_done, u * (PH // 2) + PH)
                        sp.wait_ge(xt_lo_done, u * (PH // 2))
                    sp.dma_start(xt_raw[:, :, :], xT_rows[bass.ds(u * (D // 2) + D, D), :].rearrange(
                        "(k p) n -> p k n", p=P)).then_inc(xt_in, 16)
                if at(u, UNITS - 1):
                    sp.wait_ge(xt_hi_done, PH * B)
                    sp.wait_ge(xt_lo_done, PH * (B - 1))
                    sp.dma_start(xo_of(u, k), unit_rows(x_rows, u)).then_inc(x_last_in, 16)
                if not before(u, 2):
                    sp.wait_ge(normalised, u * NT - NT)
                    store(u - 2, k)
                if at(u, UNITS - 1):
                    return
                if not before(u, 2):
                    if k % 2 == 0:
                        sp.wait_ge(stored[0], u * 8)
                    else:
                        sp.wait_ge(stored[1], u * 8 - 8)
                load_x(u, k)

            run_units(sp, unit)
            sp.wait_ge(normalised, (UNITS - 1) * NT)
            store(UNITS - 2, 0)
            for n in range(NT):
                sp.wait_ge(last_normalised, n + 1)
                r0 = (UNITS - 1) * HALF + n * P
                sp.dma_start(out_rows[r0:r0 + P, :], xo_of(UNITS - 1, 1)[:, n, :]).then_inc(stored[1], 16)
            sp.wait_ge(stored[0], 16 * B)
            sp.wait_ge(stored[1], 16 * (B - 1) + 16 * NT)

        @block.tensor
        def _(pe):
            def mm(o, l, r, start, stop):
                return nc.tensor.matmul(o, l, r, start=start, stop=stop)

            def keep_warm(count):
                for _ in range(count):
                    mm(ring[RING - 1][:, 0:P], sq[0][:, 0:P], sq[0][:, 0:P], True, True)

            pe.wait_ge(zeros_done, 1)
            keep_warm(WARM[0])
            pe.wait_ge(wqk_in, 32)
            for dt in range(KT):
                for e in range(KT):
                    last = mm(g_norm[:, dt * D:(dt + 1) * D], wq_sb[:, e, dt * P:(dt + 1) * P], wk_sb[:, e, :],
                              e == 0, e == KT - 1)
            last.then_inc(g_done, 1)
            keep_warm(WARM[1])

            def project_y(u, k):
                xh, xl = xt_hi[k // 2], xt_lo[k // 2]
                if at(u, 0):
                    pe.wait_ge(g_hi_done, 1)
                    pe.wait_ge(g_lo_done, 1)
                for i in range(PH):
                    if at(u, 0):
                        if i % KT == 0:
                            pe.wait_ge(xt_hi_done, i + KT)
                            pe.wait_ge(xt0_lo_done, i + KT)
                    else:
                        if i == 0:
                            pe.wait_ge(xt_hi_done, u * (PH // 2) + PH)
                            pe.wait_ge(xt_lo_done, u * (PH // 2))
                        free_rel(u - 1, MT - PH + i)
                    c, e = i // KT, i % KT
                    n_ = slice(c * HALF, (c + 1) * HALF)
                    e_ = slice(e * P, (e + 1) * P)
                    for d in range(KT):
                        mm(ring[i][:, :], g_hi[:, d, e_], xh[:, d, n_], d == 0, False)
                        mm(ring[i][:, :], g_hi[:, d, e_], xl[:, d, n_], False, False)
                        last = mm(ring[i][:, :], g_lo[:, d, e_], xh[:, d, n_], False, d == KT - 1)
                    last.then_inc(tile_full, 1)

            def project_v(u, k):
                xh, xl = xt_hi[k // 2], xt_lo[k // 2]
                if at(u, 1):
                    pe.wait_ge(wv_hi_done, 1)
                    pe.wait_ge(wv_lo_done, 1)
                for i in range(PH):
                    free_rel(u - 1, MT - PH + i)
                    for s in range(2):
                        m_ = slice((2 * i + s) * P, (2 * i + s + 1) * P)
                        o = ring[i][:, s * D:(s + 1) * D]
                        for d in range(KT):
                            mm(o, xh[:, d, m_], wv_hl[:, d, 0, :], d == 0, False)
                            mm(o, xh[:, d, m_], wv_hl[:, d, 1, :], False, False)
                            last = mm(o, xl[:, d, m_], wv_hl[:, d, 0, :], False, d == KT - 1)
                    last.then_inc(tile_full, 1)

            def free_rel(u, j):
                pe.wait_ge(lo_done, u * UT + (PH + j + 1))

            def norms(u, k):
                pe.wait_ge(sum_lo_done, u)
                if at(u, 1):
                    pe.wait_ge(ones_hi_done, 1)
                if not before(u, 2):
                    pe.wait_ge(diagonal_kept, u - 1)
                mm(g_norm[:, :], ones_hi[:, :], sqsum_hi[:, :], True, False)
                mm(g_norm[:, :], ones_hi[:, :], sqsum_lo[:, :], False, True).then_inc(norm_full, 1)

            def scores(u, k, j):
                if j == 0:
                    pe.wait_ge(lo_done, u * UT + KT)
                elif j < PH:
                    pe.wait_ge(lo_done, u * UT + (j + 1))
                else:
                    free_rel(u, j - PH)
                xh, xl = xt_hi[k // 2], xt_lo[k // 2]
                n_ = slice((k % 2) * HALF, (k % 2 + 1) * HALF)
                m_ = slice(j * P, (j + 1) * P)
                o = ring[j % RING][:, :]
                for d in range(KT):
                    mm(o, xh[:, d, m_], y_hi[:, d, n_], d == 0, False)
                    mm(o, xh[:, d, m_], y_lo[:, d, n_], False, False)
                    last = mm(o, xl[:, d, m_], y_hi[:, d, n_], False, d == KT - 1)
                last.then_inc(tile_full, 1)

            def rel_v(u, k, j):
                n, c, h = j // 2, j % 2, (k - 1) % 2
                last_unit = at(u, UNITS)
                o = (last_pv if last_unit else pv)[n]
                if last_unit:
                    if j < 2:
                        pe.wait_ge(lo_done, UNITS * UT - MT // 2 * (1 - j))
                elif j == 0:
                    pe.wait_ge(lo_done, u * UT + PH if k % 2 else u * UT)
                if last_unit:
                    if j == 0:
                        pe.wait_ge(pv_free, (UNITS - 2) * NT + 1)
                elif c == 0 and n == 3:
                    pe.wait_ge(pv_free, u * NT - NT + 2)
                elif c == 0 and not at(u, 1):
                    pe.wait_ge(pv_free, u * NT - 2 * NT + (1, 4, 3)[n])
                n_ = slice(n * P, (n + 1) * P)
                for m in range(c * MT // 2, (c + 1) * MT // 2):
                    hi = (o[:, :], rel_hi[h][:, m, n_], v_hl[:, m, :, :].rearrange("p a d -> p (a d)"))
                    lo = (o[:, 0:D], rel_lo[h][:, m, n_], v_hl[:, m, 0, :])
                    if m < MT - 1:
                        mm(*hi, m == 0, False)
                        mm(*lo, False, False)
                    else:
                        mm(*lo, False, False)
                        mm(*hi, False, True).then_inc(pv_full, 1)

            def unit(u, k):
                (project_v if k % 2 else project_y)(u, k)
                first = at(u, 0)
                for j in range(MT):
                    scores(u, k, j)
                    if j == 1 and not first:
                        norms(u, k)
                    if first or j == 0:
                        continue
                    rel_v(u, k, j - 1)
                if not first:
                    rel_v(u, k, MT - 1)

            run_units(pe, unit)
            for j in range(MT):
                if j == 2:
                    norms(UNITS, 0)
                rel_v(UNITS, 0, j)

        @block.scalar
        def _(act):
            def to_hi(dst, src):
                return nc.scalar.activation(dst, src, ACT.Copy)

            for i in range(PH):
                if i == KT:
                    act.wait_ge(g_done, 1)
                    to_hi(g_hi[:, :, :].rearrange("p k d -> p (k d)"), g_norm[:, :]).then_inc(g_hi_done, 1)
                if i % KT == 0:
                    act.wait_ge(xt0_in[i // KT], 16)
                to_hi(piece(xt_hi[0], i), piece(xt_raw, i)).then_inc(xt_hi_done, 1)
            act.wait_ge(wv_in, 16)
            to_hi(wv_hl[:, :, 0, :], wv_raw[:, :, :]).then_inc(wv_hi_done, 1)

            def normalise(w, kw, n):
                if n == 0:
                    act.wait_ge(shift_done, w + 1)
                t = xo[kw % 2][:, n, :]
                nc.scalar.activation(t, t, ACT.Identity, bias=shift[kw % 2][:, n:n + 1],
                                     scale=rstd[kw % 2][:, n:n + 1]).then_inc(normalised, 1)

            def split_sum(u):
                act.wait_ge(added, u * ADDS)
                if not before(u, 2):
                    act.wait_ge(norm_full, u - 1)
                to_hi(sqsum_hi[:, :], sqsum[:, :]).then_inc(sum_hi_done, 1)

            def unit(u, k):
                h = k % 2
                for i in range(PH):
                    if i == 2 and not at(u, 0):
                        split_sum(u)
                    act.wait_ge(tile_full, u * UT + (i + 1))
                    if h:
                        dst = v_hl[:, 2 * i:2 * i + 2, 0, :]
                        src = ring[i][:, :].rearrange("p (s d) -> p s d", s=2)
                    else:
                        dst, src = piece(y_hi, i), ring[i][:, :]
                    to_hi(dst, src).then_inc(hi_done, 1)
                for j in range(MT):
                    act.wait_ge(masked, u * MT + (j + 1))
                    to_hi(rel_hi[h][:, j, :], ring[j % RING][:, :]).then_inc(hi_done, 1)
                    if j == 0:
                        dst = sqsum
                        if not before(u, 1):
                            act.wait_ge(sum_lo_done, u)
                    else:
                        g = (ADDS * h + j - 1) % 2
                        dst = sq[g]
                        if not (at(u, 0) and j < 3):
                            act.wait_ge(added, u * ADDS + (j - 2))
                    nc.scalar.activation(dst[:, :], ring[j % RING][:, :], ACT.Square).then_inc(squared, 1)
                    if j == MT - 1 and not before(u, 2):
                        for n in range(NT):
                            normalise(u - 2, k, n)
                    if h and j < PH and not at(u, UNITS - 1):
                        i = j
                        if i == 0:
                            act.wait_ge(xt_in, u * 8 + 8)
                        to_hi(piece(xt_hi[(k // 2 + 1) % 2], i), piece(xt_raw, i)).then_inc(xt_hi_done, 1)

            run_units(act, unit)
            split_sum(UNITS)
            for n in range(NT):
                normalise(UNITS - 2, 0, n)

        @block.gpsimd
        def _(pool):
            nc.gpsimd.memset(ones_hi[:, :].bitcast(F32), 1.0).then_inc(ones_hi_done, 1)
            nc.gpsimd.memset(minus_half[:, :], -0.5).then_inc(minus_half_done, 1)
            nc.gpsimd.memset(diagonal[:, :, :], 0.0).then_inc(diagonal_done, 1)
            pool.wait_ge(diagonal_done, 1)
            nc.gpsimd.affine_select(out=diagonal[:, :, :], in_=diagonal[:, :, :], compare_op=ALU.not_equal,
                                    fill=1.0, base=0, pattern=[[0, NT], [-1, P]],
                                    channel_multiplier=1).then_inc(diagonal_done, 1)
            pool.wait_ge(minus_half_done, 1)

            def inverse_norm(w, kw):
                h = kw % 2
                pool.wait_ge(normsq_done, w + 1)
                nc.gpsimd.tensor_tensor(rnorm[h][:, :], normsq[h][:, :], minus_half[:, :],
                                        ALU.pow).then_inc(rnorm_done, 1)

            def inverse_deviation(w, kw, n0, n1, count):
                pool.wait_ge(var_done, count)
                nc.gpsimd.tensor_tensor(rstd[kw % 2][:, n0:n1], var_eps[:, n0:n1], minus_half[:, n0:n1],
                                        ALU.pow).then_inc(rstd_done, 1)

            def split_sum(u):
                pool.wait_ge(sum_hi_done, u + 1)
                nc.gpsimd.tensor_tensor(sqsum_lo[:, :], sqsum[:, :], sqsum_hi[:, :].bitcast(F32),
                                        ALU.subtract).then_inc(sum_lo_done, 1)

            def unit(u, k):
                h = k % 2
                for j in range(1, MT):
                    pool.wait_ge(squared, u * MT + (j + 1))
                    if not (at(u, 0) and j == 1):
                        pool.wait_ge(added, u * ADDS + (j - 1))
                    g = (ADDS * h + j - 1) % 2
                    nc.gpsimd.tensor_tensor(sqsum[:, :], sqsum[:, :], sq[g][:, :], ALU.add).then_inc(added, 1)
                    if j == 3 and not at(u, 0):
                        inverse_norm(u - 1, (k - 1) % BODY)
                    if j == 3 and not before(u, 2):
                        inverse_deviation(u - 2, (k - 2) % BODY, 0, NT, u - 1)
                    if h and j in (1, 2, 4, 5) and not at(u, UNITS - 1):
                        i = (1, 2, 4, 5).index(j)
                        nb = (k // 2 + 1) % 2
                        pool.wait_ge(xt_hi_done, u * 2 + (PH - 2 + i + 1))
                        nc.gpsimd.tensor_tensor(piece(xt_lo[nb], i), piece(xt_raw, i),
                                                piece(xt_hi[nb], i).bitcast(F32),
                                                ALU.subtract).then_inc(xt_lo_done, 1)
                split_sum(u)

            run_units(pool, unit)
            inverse_deviation(UNITS - 2, 0, 0, NT, UNITS - 1)
            inverse_norm(UNITS - 1, 1)
            inverse_deviation(UNITS - 1, 1, 0, 2, UNITS)
            inverse_deviation(UNITS - 1, 1, 2, 3, UNITS + 1)
            inverse_deviation(UNITS - 1, 1, 3, 4, UNITS + 2)

        @block.vector
        def _(dve):
            def to_lo(dst, src, hi):
                return nc.vector.tensor_tensor(dst, src, hi.bitcast(F32), ALU.subtract)

            nc.vector.memset(sq[0][:, :], 0.0).then_inc(zeros_done, 1)
            nc.vector.memset(own_sum[:, :, :], 0.0).then_inc(zeros_done, 1)
            for i in range(PH):
                if i == KT:
                    dve.wait_ge(g_hi_done, 1)
                    to_lo(g_lo[:, :, :].rearrange("p k d -> p (k d)"), g_norm[:, :],
                          g_hi[:, :, :].rearrange("p k d -> p (k d)")).then_inc(g_lo_done, 1)
                dve.wait_ge(xt_hi_done, i + 1)
                to_lo(piece(xt_lo[0], i), piece(xt_raw, i), piece(xt_hi[0], i)).then_inc(xt0_lo_done, 1)
            dve.wait_ge(wv_hi_done, 1)
            to_lo(wv_hl[:, :, 1, :], wv_raw[:, :, :], wv_hl[:, :, 0, :]).then_inc(wv_lo_done, 1)

            def mask(u, k, j):
                if at(u, 0):
                    dve.wait_ge(adj_in[j], 16)
                dve.wait_ge(tile_full, u * UT + (PH + j + 1))
                t = ring[j % RING][:, :]
                nc.vector.tensor_tensor(t, t, adj_sb[:, j, (k % 2) * HALF:(k % 2 + 1) * HALF],
                                        ALU.mult).then_inc(masked, 1)

            def phase_lo(u, k, i):
                dve.wait_ge(hi_done, u * UT + (i + 1))
                if k % 2:
                    v = v_hl[:, 2 * i:2 * i + 2, :, :]
                    ins = to_lo(v[:, :, 1, :], ring[i][:, :].rearrange("p (s d) -> p s d", s=2), v[:, :, 0, :])
                else:
                    ins = to_lo(piece(y_lo, i), ring[i][:, :], piece(y_hi, i))
                ins.then_inc(lo_done, 1)

            def rel_split(u, k, j):
                dve.wait_ge(squared, u * MT + (j + 1))
                h = k % 2
                to_lo(rel_lo[h][:, j, :], ring[j % RING][:, :], rel_hi[h][:, j, :]).then_inc(lo_done, 1)

            def rel_v_bank(w, n):
                return (last_pv if at(w, UNITS - 1) else pv)[n]

            def keep_diagonal(w):
                t = g_norm[:, :].rearrange("p (t n) -> p t n", t=NT)
                nc.vector.copy_predicated(own_sum[:, :, :], diagonal[:, :, :].bitcast(mybir.dt.uint32),
                                          t).then_inc(diagonal_kept, 1)

            def norm_squares(w, kw):
                dve.wait_ge(diagonal_kept, w + 1)
                nc.vector.tensor_reduce(normsq[kw % 2][:, :], own_sum[:, :, :],
                                        mybir.AxisListType.X, ALU.add).then_inc(normsq_done, 1)

            def add_x(w, kw, n):
                h = kw % 2
                dve.wait_ge(pv_full, w * NT + (n + 1))
                if n == 0:
                    dve.wait_ge(rnorm_done, w + 1)
                    if at(w, UNITS - 1):
                        dve.wait_ge(x_last_in, 16)
                    else:
                        dve.wait_ge(x_in[h], w * 8 + (8 if h else 16))
                t = xo_of(w, kw)[:, n, :]
                nc.vector.scalar_tensor_tensor(t, rel_v_bank(w, n)[:, 0:D], rnorm[h][:, n:n + 1], t,
                                               ALU.mult, ALU.add).then_inc(x_added, 1)

            def add_cross(w, kw, n):
                h = kw % 2
                dve.wait_ge(x_added, w * NT + (n + 1))
                t = xo_of(w, kw)[:, n, :]
                nc.vector.scalar_tensor_tensor(t, rel_v_bank(w, n)[:, D:2 * D], rnorm[h][:, n:n + 1], t,
                                               ALU.mult, ALU.add).then_inc(pv_free, 1)

            def tile_stats(w, kw, n):
                dve.wait_ge(pv_free, w * NT + (n + 1))
                nc.vector.bn_stats(stats[n % 2][:, :], xo_of(w, kw)[:, n, :]).then_inc(stats_done, 1)

            def tile_aggr(w, kw, n):
                nc.vector.bn_aggr(meanvar[kw % 2][:, n, :], stats[n % 2][:, :]).then_inc(aggr_done, 1)

            def variance(w, kw, n0, n1):
                dve.wait_ge(aggr_done, w * NT + n1)
                nc.vector.tensor_scalar_add(var_eps[:, n0:n1], meanvar[kw % 2][:, n0:n1, 1],
                                            EPS).then_inc(var_done, 1)

            def shift_of(w, kw):
                h = kw % 2
                dve.wait_ge(rstd_done, w + 1)
                nc.vector.scalar_tensor_tensor(shift[h][:, :], meanvar[h][:, :, 0], -1.0, rstd[h][:, :],
                                               ALU.mult, ALU.mult).then_inc(shift_done, 1)

            def last_normalise(w, kw, n):
                dve.wait_ge(rstd_done, w + max(n, 1))
                t = xo_of(w, kw)[:, n, :]
                nc.vector.tensor_scalar(t, t, meanvar[kw % 2][:, n, 0:1], rstd[kw % 2][:, n:n + 1],
                                        ALU.subtract, ALU.mult).then_inc(last_normalised, 1)

            def unit(u, k):
                one = at(u, 0)
                two = at(u, 1)
                p, kp = u - 1, (k - 1) % BODY
                q, kq = u - 2, (k - 2) % BODY
                has_p, has_q = not one, not (one or two)
                for i in range(PH):
                    phase_lo(u, k, i)
                    if has_q and i == 0:
                        add_x(q, kq, 2)
                    elif has_q and i == 1:
                        add_cross(q, kq, 2)
                    elif has_q and i == 2:
                        tile_stats(q, kq, 2)
                if has_q:
                    dve.wait_ge(stats_done, q * NT + 3)
                for j in range(MT):
                    if has_p and j == 3:
                        dve.wait_ge(norm_full, p + 1)
                    mask(u, k, j)
                    if has_q and j == 0:
                        tile_aggr(q, kq, 2)
                        add_x(q, kq, 3)
                    elif has_q and j == 1:
                        add_cross(q, kq, 3)
                    elif has_q and j == 2:
                        tile_stats(q, kq, 3)
                        dve.wait_ge(stats_done, q * NT + 4)
                    elif has_p and j == 3:
                        keep_diagonal(p)
                    elif has_p and j in (5, 6):
                        add_x(p, kp, j - 5)
                    elif has_p and j == 7:
                        tile_stats(p, kp, 0)
                    if j > 0:
                        rel_split(u, k, j - 1)
                    if has_q and j == 2:
                        tile_aggr(q, kq, 3)
                    elif has_p and j == 3:
                        norm_squares(p, kp)
                        if has_q:
                            variance(q, kq, 0, NT)
                    elif has_p and j in (5, 6):
                        add_cross(p, kp, j - 5)
                        if has_q and j == 6:
                            shift_of(q, kq)
                    elif has_p and j == 7:
                        tile_stats(p, kp, 1)
                        dve.wait_ge(stats_done, p * NT + 2)
                rel_split(u, k, MT - 1)
                if has_p:
                    tile_aggr(p, kp, 0)
                    tile_aggr(p, kp, 1)

            dve.wait_ge(zeros_done, 2)
            dve.wait_ge(diagonal_done, 2)
            run_units(dve, unit)
            q, kq = UNITS - 2, (UNITS - 2) % BODY
            for n in (2, 3):
                add_x(q, kq, n)
                add_cross(q, kq, n)
                tile_stats(q, kq, n)
                dve.wait_ge(stats_done, q * NT + n + 1)
                tile_aggr(q, kq, n)
            variance(q, kq, 0, NT)
            p, kp = UNITS - 1, (UNITS - 1) % BODY
            dve.wait_ge(norm_full, p + 1)
            keep_diagonal(p)
            norm_squares(p, kp)
            shift_of(q, kq)
            def both(step, n0, n1):
                step(p, kp, n0)
                step(p, kp, n1)

            both(add_x, 0, 1)
            both(add_cross, 0, 1)
            both(tile_stats, 0, 1)
            dve.wait_ge(stats_done, p * NT + 2)
            both(tile_aggr, 0, 1)
            variance(p, kp, 0, 2)
            add_x(p, kp, 2)
            add_cross(p, kp, 2)
            both(last_normalise, 0, 1)
            tile_stats(p, kp, 2)
            dve.wait_ge(stats_done, p * NT + 3)
            tile_aggr(p, kp, 2)
            variance(p, kp, 2, 3)
            add_x(p, kp, 3)
            add_cross(p, kp, 3)
            last_normalise(p, kp, 2)
            tile_stats(p, kp, 3)
            dve.wait_ge(stats_done, p * NT + 4)
            tile_aggr(p, kp, 3)
            variance(p, kp, 3, 4)
            last_normalise(p, kp, 3)


def kernel(x, adj, L0_gnn_Wq, L0_gnn_Wk, L0_gnn_Wv):
    import concourse.bacc as bacc
    from concourse.bass_utils import run_bass_kernel_spmd

    nc = bacc.Bacc("TRN2", target_bir_lowering=False, num_devices=1)
    x = np.ascontiguousarray(x)
    arrays = {
        "x": x,
        "xT": np.ascontiguousarray(x.transpose(0, 2, 1)),
        "adj": np.ascontiguousarray(adj),
        "wq": np.ascontiguousarray(L0_gnn_Wq),
        "wk": np.ascontiguousarray(L0_gnn_Wk),
        "wvT": np.ascontiguousarray(np.asarray(L0_gnn_Wv).T),
    }
    args = [nc.dram_tensor(name, a.shape, F32, kind="ExternalInput").ap() for name, a in arrays.items()]
    out = nc.dram_tensor("out", x.shape, F32, kind="ExternalOutput").ap()
    build(nc, *args, out)
    r = run_bass_kernel_spmd(nc, [arrays], core_ids=[0])
    return r.results[0]["out"]
```
